# Optimizing a Trainium2 kernel written in Bass

```python
import numpy as np
import jax
import jax.numpy as jnp

def _softmax(x, axis=-1):
    return jax.nn.softmax(x, axis=axis)

def _gelu(x):
    return jax.nn.gelu(x, approximate=True)

def _silu(x):
    return jax.nn.silu(x)

def _sigmoid(x):
    return jax.nn.sigmoid(x)

def _layernorm(x, axis=-1, eps=1e-05):
    m = jnp.mean(x, axis=axis, keepdims=True)
    v = jnp.var(x, axis=axis, keepdims=True)
    return (x - m) / jnp.sqrt(v + eps)

def _scatter_add(tgt, idx, src, axis=0):
    return tgt.at[idx].add(src)

def _segment_sum(src, seg, n):
    return jax.ops.segment_sum(src, seg, n)
kernel_name = 'mk_gnn_resnorm_d1_gnn_r64_49299e'

def setup_inputs(seed: int=0):
    np.random.seed(seed)
    _w = jnp.asarray

    def _rec_inputs():
        import jax
        import jax.numpy as jnp
        _gk = jax.random.key(seed)
        x = -0.0001006 + 1 * jax.random.normal(jax.random.fold_in(_gk, 1), (100000, 96), jnp.float32)
        src = jax.random.randint(jax.random.fold_in(_gk, 2), (50000,), 0, 100000, jnp.int32)
        dst = jnp.minimum((100000 * jax.random.uniform(jax.random.fold_in(_gk, 3), (50000,)) ** 2.0).astype(jnp.int32), 99999)
        _o = jnp.argsort(dst, stable=True)
        src = src[_o]
        dst = dst[_o]
        return (x, src, dst)
    x, src, dst = _rec_inputs()

    def _L0_gnn_setup():
        import jax, jax.numpy as jnp
        import numpy as np
        N_NODES = 50000
        N_EDGES = 12500
        D_IN = 96
        D_OUT = 96
        key = jax.random.key(seed)
        k1, k2, k3, k4 = jax.random.split(key, 4)
        x = jax.random.normal(k1, (N_NODES, D_IN), dtype=jnp.float32)
        edge_index = jax.random.randint(k2, (2, N_EDGES), 0, N_NODES, dtype=jnp.int64)
        W = jax.random.normal(k3, (D_IN, D_OUT), dtype=jnp.float32) * (1.0 / np.sqrt(D_IN))
        b = jax.random.normal(k4, (D_OUT,), dtype=jnp.float32) * 0.01
        return {'x': x, 'edge_index': edge_index, 'W': W, 'b': b}
    _L0_gnn_all = _L0_gnn_setup()
    _L0_gnn_in = {k: v for k, v in _L0_gnn_all.items() if k in ('W', 'b')}
    del _L0_gnn_all
    return {'x': x, 'src': src, 'dst': dst, 'L0_gnn_W': _L0_gnn_in['W'], 'L0_gnn_b': _L0_gnn_in['b']}

def reference(x, src, dst, L0_gnn_W, L0_gnn_b):
    import jax
    import jax.numpy as jnp

    def _L0_gnn_ref(x, edge_index, W, b):
        import jax, jax.numpy as jnp
        import numpy as np
        N_NODES = 50000
        N_EDGES = 12500
        D_IN = 96
        D_OUT = 96
        num_nodes = x.shape[0]
        src, dst = (edge_index[0], edge_index[1])
        messages = x[src] @ W + b
        out = jax.ops.segment_sum(messages, dst, num_segments=num_nodes)
        deg = jax.ops.segment_sum(jnp.ones((dst.shape[0],), dtype=x.dtype), dst, num_segments=num_nodes)
        deg = jnp.clip(deg, 1.0, None)
        return out / deg[:, None]
    edge_index = jnp.stack([src, dst])
    x = _layernorm(x + _L0_gnn_ref(x, edge_index, L0_gnn_W, L0_gnn_b), axis=-1)
    return x

_drawn_inputs = setup_inputs


def setup_inputs(seed=0):
    import zlib

    import numpy as np

    out = dict(_drawn_inputs(seed))
    spreads = {}
    factors = {'L0_gnn_b': 8.0}
    for name, (base, spread) in spreads.items():
        noise = np.random.default_rng([zlib.crc32(name.encode()), seed]).standard_normal(out[name].shape)
        drawn = base * np.exp(spread * noise) if base else spread * noise
        out[name] = jnp.asarray(drawn.astype(out[name].dtype))
    for name, factor in factors.items():
        out[name] = (out[name] * factor).astype(out[name].dtype)
    return out
```

```python
import concourse.bass as bass
from concourse import mybir
from contextlib import ExitStack


def gnn_residual_layernorm(nc, x, src, dst, W, b, out):
    fp32 = mybir.dt.float32
    i32 = mybir.dt.int32
    ALU = mybir.AluOpType
    ACT = mybir.ActivationFunctionType

    P = 128
    N, D = x.shape
    E = src.shape[0]
    D1 = D + 1
    EPS = 1e-5

    ROW = 512
    NROW = -(-E // ROW)
    TPR = ROW // P
    NT = NROW * TPR
    EDGES_LAST_ROW = E - (NROW - 1) * ROW
    U = 14
    NI = NT // U
    LAG = 8
    RELAY = 3
    assert NI * U == NT

    G = 32
    SHIFT = 12
    SUPER = P * G
    assert SUPER == 1 << SHIFT
    NS = N // SUPER
    REST = N - NS * SUPER
    GR = REST // P
    R1 = REST - GR * P
    SL = 4
    PAD_DST = float(1 << 20)
    PAD_NEXT = float(1 << 21)
    SKIP = float(1 << 22)

    zero_chunks = NS + 1
    ZS = 4

    agg = nc.dram_tensor("agg", (N, D), fp32, kind="Internal").ap()

    with ExitStack() as ctx:
        def sb(name, shape, dt=fp32):
            return ctx.enter_context(nc.sbuf_tensor(name, shape, dt))

        def pb(name, shape):
            return ctx.enter_context(nc.psum_tensor(name, shape, fp32))

        def sem(name):
            return ctx.enter_context(nc.semaphore(name))

        src_row = sb("src_row", [NROW, ROW], i32)
        dst_row = sb("dst_row", [NROW, ROW], i32)
        next_row = sb("next_row", [NROW, ROW], i32)
        src_rowf = sb("src_rowf", [NROW, ROW])
        dst_rowf = sb("dst_rowf", [NROW, ROW])
        next_rowf = sb("next_rowf", [NROW, ROW])
        gather_idx = sb("gather_idx", [P, NT], i32)
        scatter_idx = sb("scatter_idx", [P, NT], i32)
        now_gather = sb("now_gather", [P, 2 * U], i32)
        now_scatter = sb("now_scatter", [P, 2 * U], i32)
        dst_col = sb("dst_col", [P, NT])
        prev_last = sb("prev_last", [P, NT])
        plan_raw = sb("plan_raw", [1, 2, NI + 1], i32)
        plan = sb("plan", [1, 2, NI + 1], i32)
        ident = sb("ident", [P, P])
        ones = sb("ones", [P, P])
        zeros = sb("zeros", [P, G * D])
        last_only = sb("last_only", [P, 2])
        w1 = sb("w1", [D1, D1])
        xg = sb("xg", [P, U, D1])
        xT = sb("xT", [D1, 2, P])
        diag = sb("diag", [P, 2, P])
        msg = sb("msg", [P, 2, D1])
        same = sb("same", [P, 2, P])
        carry = sb("carry", [P, 2, P])
        seg = sb("seg", [P, U, D1])
        deg = sb("deg", [P, U])
        rdeg = sb("rdeg", [P, U])
        mean = sb("mean", [P, U, D])
        xs = sb("xs", [P, SL, G * D])
        ag = sb("ag", [P, SL, G * D])
        stats = sb("stats", [P, G, 6])
        tmp = sb("tmp", [P, 6, G])

        ps_tab = [pb(f"ps_tab{i}", [P, 512]) for i in range(1)]
        ps_xT = pb("ps_xT", [P, 512])
        ps_msg = pb("ps_msg", [P, 512])
        ps_dst = [pb(f"ps_dst{i}", [P, 512]) for i in range(2)]
        ps_seg = [pb(f"ps_seg{i}", [P, 512]) for i in range(2)]

        pads_set = sem("pads_set")
        rows_loaded = sem("rows_loaded")
        w_loaded = sem("w_loaded")
        w_zeroed = sem("w_zeroed")
        ident_zero = sem("ident_zero")
        ident_ready = sem("ident_ready")
        consts_ready = sem("consts_ready")
        rows_ready = sem("rows_ready")
        tabs_T = sem("tabs_T")
        tabs_copied = sem("tabs_copied")
        plan_ready = sem("plan_ready")
        setup = sem("setup")
        zero_landed = [sem(f"zero_landed{i}") for i in range(ZS)]
        zeroed = sem("zeroed")
        gathered = [sem(f"gathered{i}") for i in range(U)]
        scattered = [sem(f"scattered{i}") for i in range(U)]
        scatters_done = sem("scatters_done")
        now_ready = sem("now_ready")
        xT_ready = sem("xT_ready")
        xT_copied = sem("xT_copied")
        msg_ready = sem("msg_ready")
        msg_copied = sem("msg_copied")
        diag_ready = sem("diag_ready")
        dst_ready = sem("dst_ready")
        masks_ready = sem("masks_ready")
        seg_ready = sem("seg_ready")
        seg_copied = sem("seg_copied")
        deg_ready = sem("deg_ready")
        mean_ready = sem("mean_ready")
        super_loaded = sem("super_loaded")
        super_chain = sem("super_chain")
        var_ready = sem("var_ready")
        std_ready = sem("std_ready")
        normed = sem("normed")
        stored = sem("stored")
        sp_passed = sem("sp_passed")
        pool_passed = sem("pool_passed")
        dve_passed = sem("dve_passed")
        rest_loaded = sem("rest_loaded")
        rest_stored = sem("rest_stored")

        block = ctx.enter_context(nc.Block())

        ROW_DMAS = 8
        LINKS = 7

        def src_or_dst(row):
            return src if row is src_row else dst

        def nodes(a, k):
            return a[bass.ds(k * SUPER, SUPER), :].rearrange("(p g) d -> p (g d)", g=G)

        def held_wait(eng, what, count, passed):
            eng.wait_ge(what, count)
            eng.sem_inc(passed, 1)

        @block.sync
        def _(sp):
            sp.wait_ge(pads_set, 3)
            full = (NROW - 1) * ROW
            for row, first, count in ((src_row, 0, E), (dst_row, 0, E), (next_row, 1, E - 1)):
                sp.dma_start(row[0:NROW - 1, :], src_or_dst(row)[first:first + full].rearrange(
                    "(q j) -> q j", j=ROW)).then_inc(rows_loaded, 16)
                sp.dma_start(row[NROW - 1:NROW, 0:count - full],
                             src_or_dst(row)[None, first + full:first + count]).then_inc(rows_loaded, 16)
            stride = U * P
            first_at = (U - LAG) * P
            last_at = (U - LAG) * P - 1
            with nc.allow_non_contiguous_dma(reason="a few single values"):
                sp.dma_start(plan_raw[0:1, 0, 1:NI],
                             dst[first_at:first_at + stride * (NI - 2) + 1:stride][None, :]).then_inc(rows_loaded, 16)
                sp.dma_start(plan_raw[0:1, 1, 0:NI],
                             dst[last_at:last_at + stride * (NI - 1) + 1:stride][None, :]).then_inc(rows_loaded, 16)
            sp.wait_ge(w_zeroed, 1)
            sp.dma_start(w1[0:D, 0:D], W[:, :]).then_inc(w_loaded, 16)
            sp.dma_start(w1[D:D1, 0:D], b[None, :]).then_inc(w_loaded, 16)

            sp.wait_ge(consts_ready, 1)
            for j in range(zero_chunks):
                if j < NS:
                    sp.dma_start(nodes(agg, j), zeros[:, :]).then_inc(zero_landed[j % ZS], 16)
                else:
                    sp.dma_start(agg[NS * SUPER:NS * SUPER + GR * P, :].rearrange("(p g) d -> p (g d)", g=GR),
                                 zeros[:, 0:GR * D]).then_inc(zero_landed[j % ZS], 16)
                if j >= ZS - 1:
                    sp.wait_ge(zero_landed[(j - ZS + 1) % ZS], 16 * ((j - ZS + 1) // ZS + 1))
                    sp.sem_inc(zeroed, 1)
            for j in range(zero_chunks - ZS + 1, zero_chunks):
                sp.wait_ge(zero_landed[j % ZS], 16 * (j // ZS + 1))
                if j < zero_chunks - 1:
                    sp.sem_inc(zeroed, 1)
            last = zero_chunks % ZS
            sp.dma_start(agg[NS * SUPER + GR * P:N, :], zeros[0:R1, 0:D]).then_inc(zero_landed[last], 16)
            sp.wait_ge(zero_landed[last], 16 * (zero_chunks // ZS + 1))
            sp.sem_inc(zeroed, 1)

            def load(k):
                sp.dma_start(xs[:, k & (SL - 1), :], nodes(x, k)).then_inc(super_loaded, 16)
                sp.dma_start(ag[:, k & (SL - 1), :], nodes(agg, k)).then_inc(super_loaded, 16)
                held_wait(sp, super_loaded, 32 * k + 32, sp_passed)

            def store(k):
                if isinstance(k, int):
                    sp.wait_ge(stored, 16 * k)
                else:
                    with sp.If(k > 0):
                        held_wait(sp, stored, 16 * k, sp_passed)
                held_wait(sp, normed, k + 1, sp_passed)
                sp.dma_start(nodes(out, k), xs[:, k & (SL - 1), :]).then_inc(stored, 16)

            sp.wait_ge(plan_ready, 1)

            def supers(c, done):
                lo = sp.value_load(plan[0:1, 0, bass.ds(c, 1)], min_val=0, max_val=NS)
                hi = sp.value_load(plan[0:1, 0, bass.ds(c + 1, 1)], min_val=0, max_val=NS)
                held_wait(sp, scatters_done, done, sp_passed)
                with sp.If(lo < hi):
                    with sp.Fori(lo, hi) as k:
                        load(k)
                        with sp.If(k > 0):
                            store(nc.s_assert_within((k - 1) & 31, 0, NS - 1, skip_runtime_bounds_check_because="k > 0 here"))

            with sp.Fori(0, NI - 1) as i:
                supers(i, i * U + (U - LAG))
            supers(NI - 1, NT)
            base = NS * SUPER
            r = NS & (SL - 1)
            for buf, a in ((xs, x), (ag, agg)):
                sp.dma_start(buf[:, r, 0:GR * D], a[base:base + GR * P, :].rearrange(
                    "(p g) d -> p (g d)", g=GR)).then_inc(rest_loaded, 16)
                sp.dma_start(buf[0:R1, r, GR * D:(GR + 1) * D], a[base + GR * P:N, :]).then_inc(rest_loaded, 16)
            store(NS - 1)
            sp.wait_ge(normed, NS + 1)
            sp.dma_start(out[base:base + GR * P, :].rearrange("(p g) d -> p (g d)", g=GR),
                         xs[:, r, 0:GR * D]).then_inc(rest_stored, 16)
            sp.dma_start(out[base + GR * P:N, :], xs[0:R1, r, GR * D:(GR + 1) * D]).then_inc(rest_stored, 16)
            sp.wait_ge(stored, 16 * NS)
            sp.wait_ge(rest_stored, 32)

        @block.gpsimd
        def _(pool):
            nc.gpsimd.memset(ident[:, :], 0.0).then_inc(ident_zero, 1)
            nc.gpsimd.memset(last_only[:, 0:1], 0.0).then_inc(ident_zero, 1)
            pool.wait_ge(ident_zero, 2)
            nc.gpsimd.affine_select(out=ident[:, :], in_=ident[:, :], compare_op=ALU.not_equal, fill=1.0,
                                    base=0, pattern=[[-1, P]], channel_multiplier=1).then_inc(ident_ready, 1)
            nc.gpsimd.affine_select(out=last_only[:, 0:1], in_=last_only[:, 0:1], compare_op=ALU.not_equal,
                                    fill=1.0, base=-(P - 1), pattern=[[0, 1]],
                                    channel_multiplier=1).then_inc(ident_ready, 1)
            pool.wait_ge(tabs_copied, 3 * TPR)
            pool.wait_ge(plan_ready, 1)
            pool.wait_ge(consts_ready, 2)

            def gather(t, u, c):
                pool.indirect_dma_start(
                    out=xg[:, u, 0:D], out_offset=None, in_=x[:, :],
                    in_offset=bass.IndirectOffsetOnAxis(ap=now_gather[:, c:c + 1], axis=0),
                ).then_inc(gathered[u], 16)

            def scatter(t, u, c):
                held_wait(pool, mean_ready, t + 1, pool_passed)
                pool.indirect_dma_start(
                    out=agg[:, :], out_offset=bass.IndirectOffsetOnAxis(ap=now_scatter[:, c:c + 1], axis=0),
                    in_=mean[:, u, :], in_offset=None, bounds_check=N - 1, oob_is_err=False,
                ).then_inc(scattered[u], 16)

            def relay(u, turn):
                pool.wait_ge(scattered[u], 16 * turn)
                pool.sem_inc(scatters_done, 1)

            def zeroed_for(i):
                need = pool.value_load(plan[0:1, 1, bass.ds(i, 1)], min_val=0, max_val=NS)
                held_wait(pool, zeroed, need + 1, pool_passed)

            def stage(j, bank):
                if not (isinstance(j, int) and j < 2):
                    held_wait(pool, xT_ready, (j - 1) * U, pool_passed)
                cols = slice(bank * U, (bank + 1) * U)
                nc.gpsimd.tensor_copy(now_gather[:, cols], gather_idx[:, bass.ds(j * U, U)]).then_inc(now_ready, 1)
                nc.gpsimd.tensor_copy(now_scatter[:, cols], scatter_idx[:, bass.ds(j * U, U)]).then_inc(now_ready, 1)
                held_wait(pool, now_ready, 2 * j + 2, pool_passed)

            def body(i):
                first = isinstance(i, int)
                for h in range(2):
                    j = i * 2 + h
                    stage(j, h)
                    zeroed_for(j)
                    for u in range(U):
                        c = h * U + u
                        if not (first and h == 0):
                            held_wait(pool, xT_ready, j * U + (u - U + 1), pool_passed)
                        gather(j * U + u, u, c)
                        if not first or c >= LAG:
                            scatter(j * U + (u - LAG), (u - LAG) % U, (c - LAG) % (2 * U))
                        if not first or c >= LAG + RELAY:
                            v = c - LAG - RELAY
                            relay(v % U, i * 2 + 1 + v // U)

            body(0)
            with pool.Fori(1, NI // 2) as i:
                body(i)
            pool.wait_ge(zeroed, zero_chunks)
            for t in range(NT - LAG, NT):
                scatter(t, t % U, t % (2 * U))
            for t in range(NT - LAG - RELAY, NT):
                relay(t % U, t // U + 1)

        @block.tensor
        def _(pe):
            pe.wait_ge(ident_ready, 2)
            pe.wait_ge(rows_ready, 3)
            n = 0
            for rows in (src_rowf, next_rowf, dst_rowf):
                for g in range(TPR):
                    if n:
                        pe.wait_ge(tabs_copied, n)
                    nc.tensor.transpose(ps_tab[0][:, 0:NROW], rows[:, g * P:(g + 1) * P],
                                        ident[0:NROW, 0:NROW]).then_inc(tabs_T, 1)
                    n += 1

            def transpose(t, u):
                pe.wait_ge(gathered[u], 16 * (t // U + 1) if isinstance(t, int) else 16 * t[0] + 16)
                tt = t if isinstance(t, int) else t[0] * U + u
                if not (isinstance(t, int) and t == 0):
                    pe.wait_ge(xT_copied, tt)
                nc.tensor.transpose(ps_xT[0:D1, 0:P], xg[:, u, :], ident[:, :]).then_inc(xT_ready, 1)

            def spread(t, u):
                pe.wait_ge(diag_ready, t + 1)
                if not (isinstance(t, int) and t < 2):
                    pe.wait_ge(masks_ready, t - 1)
                nc.tensor.matmul(ps_dst[u % 2][:, 0:P], ones[:, :], diag[:, u % 2, :],
                                 start=True, stop=True).then_inc(dst_ready, 1)

            def messages(t, u):
                pe.wait_ge(xT_copied, t + 1)
                if not (isinstance(t, int) and t == 0):
                    pe.wait_ge(msg_copied, t)
                nc.tensor.matmul(ps_msg[:, 0:D1], xT[:, u % 2, :], w1[:, :],
                                 start=True, stop=True).then_inc(msg_ready, 1)

            def segments(t, u):
                pe.wait_ge(masks_ready, t + 1)
                pe.wait_ge(msg_copied, t + 1)
                nc.tensor.matmul(ps_seg[u % 2][:, 0:D1], same[:, u % 2, :], msg[:, u % 2, :],
                                 start=True, stop=False)
                if not (isinstance(t, int) and t == 0):
                    pe.wait_ge(seg_copied, t)
                nc.tensor.matmul(ps_seg[u % 2][:, 0:D1], carry[:, u % 2, :], seg[:, (u - 1) % U, :],
                                 start=False, stop=True).then_inc(seg_ready, 1)

            pe.wait_ge(consts_ready, 2)
            pe.wait_ge(w_loaded, 32)
            transpose(0, 0)
            spread(0, 0)

            def step(i, last=False):
                for u in range(U):
                    t = i * U + u
                    messages(t, u)
                    if u + 1 < U:
                        transpose(t + 1 if isinstance(i, int) else (i, 0), u + 1)
                        spread(t + 1, u + 1)
                    elif not last:
                        transpose(t + 1 if isinstance(i, int) else (i + 1, 0), 0)
                        spread(t + 1, 0)
                    segments(t, u)

            step(0)
            with pe.Fori(1, NI - 1) as i:
                step(i)
            step(NI - 1, last=True)

        @block.scalar
        def _(act):
            act.wait_ge(tabs_copied, 3 * TPR)

            def build_diag(t, u):
                if not (isinstance(t, int) and t < 2):
                    act.wait_ge(dst_ready, t - 1)
                nc.scalar.activation(diag[:, u % 2, :], ident[:, :], ACT.Copy,
                                     scale=dst_col[:, bass.ds(t, 1)]).then_inc(diag_ready, 1)

            def copy_xT(t, u):
                act.wait_ge(xT_ready, t + 1)
                if not (isinstance(t, int) and t < 2):
                    act.wait_ge(msg_ready, t - 1)
                nc.scalar.copy(xT[:, u % 2, :], ps_xT[0:D1, 0:P]).then_inc(xT_copied, 1)

            def copy_msg(t, u):
                act.wait_ge(msg_ready, t + 1)
                if not (isinstance(t, int) and t < 2):
                    act.wait_ge(seg_ready, t - 1)
                nc.scalar.copy(msg[:, u % 2, :], ps_msg[:, 0:D1]).then_inc(msg_copied, 1)

            def copy_seg(t, u):
                act.wait_ge(seg_ready, t + 1)
                if not (isinstance(t, int) and t < U):
                    act.wait_ge(mean_ready, t - U + 1)
                nc.scalar.copy(seg[:, u, :], ps_seg[u % 2][:, 0:D1]).then_inc(seg_copied, 1)

            build_diag(0, 0)
            copy_xT(0, 0)

            def step(i, last=False):
                for u in range(U):
                    t = i * U + u
                    if not (last and u == U - 1):
                        build_diag(t + 1, (u + 1) % U)
                    copy_msg(t, u)
                    if not (last and u == U - 1):
                        copy_xT(t + 1, (u + 1) % U)
                    copy_seg(t, u)
                supers(i)

            def deviation(k, groups):
                act.wait_ge(var_ready, k + 1)
                nc.scalar.activation(tmp[:, 5, 0:groups], tmp[:, 4, 0:groups], ACT.Sqrt).then_inc(std_ready, 1)

            def supers(c):
                lo = act.value_load(plan[0:1, 0, bass.ds(c, 1)], min_val=0, max_val=NS)
                hi = act.value_load(plan[0:1, 0, bass.ds(c + 1, 1)], min_val=0, max_val=NS)
                with act.If(lo < hi):
                    with act.Fori(lo, hi) as k:
                        deviation(k, G)

            act.wait_ge(plan_ready, 1)
            step(0)
            with act.Fori(1, NI - 1) as i:
                step(i)
            step(NI - 1, last=True)
            deviation(NS, GR + 1)

        @block.vector
        def _(dve):
            v = nc.vector
            v.memset(src_row[:, :], 0).then_inc(pads_set, 1)
            v.memset(dst_row[:, :], int(PAD_DST)).then_inc(pads_set, 1)
            v.memset(next_row[:, :], int(PAD_NEXT)).then_inc(pads_set, 1)
            v.memset(w1[:, :], 0.0).then_inc(setup, 1)
            dve.wait_ge(setup, 1)
            v.memset(w1[D:D1, D:D1], 1.0).then_inc(w_zeroed, 1)
            v.memset(zeros[:, :], 0.0).then_inc(consts_ready, 1)
            v.memset(ones[:, :], 1.0)
            v.memset(plan[:, :, :], 0)
            v.memset(xg[:, :, D:D1], 1.0)
            v.memset(seg[:, U - 1, :], 0.0).then_inc(consts_ready, 1)
            dve.wait_ge(rows_loaded, 16 * ROW_DMAS)
            v.tensor_copy(src_rowf[:, :], src_row[:, :]).then_inc(rows_ready, 1)
            v.tensor_copy(dst_rowf[:, :], dst_row[:, :]).then_inc(rows_ready, 1)
            dve.wait_ge(rows_ready, 2)
            v.tensor_tensor(next_rowf[:, :], dst_row[:, :], next_row[:, :], ALU.is_equal).then_inc(setup, 1)
            dve.wait_ge(setup, 2)
            v.scalar_tensor_tensor(out=next_rowf[:, :], in0=next_rowf[:, :], scalar=SKIP, in1=dst_rowf[:, :],
                                   op0=ALU.mult, op1=ALU.add).then_inc(rows_ready, 1)
            v.tensor_scalar(plan[:, 0, 1:NI], plan_raw[:, 0, 1:NI], SHIFT, None, ALU.logical_shift_right)
            v.tensor_scalar(plan[:, 1, 0:NI], plan_raw[:, 1, 0:NI], SHIFT, None, ALU.logical_shift_right)
            v.memset(plan[:, 0, NI:NI + 1], NS).then_inc(plan_ready, 1)
            n = 0
            for tab in (gather_idx, scatter_idx, dst_col):
                for g in range(TPR):
                    dve.wait_ge(tabs_T, n + 1)
                    v.tensor_copy(tab[:, g:NT:TPR], ps_tab[0][:, 0:NROW]).then_inc(tabs_copied, 1)
                    n += 1
            dve.wait_ge(ident_ready, 2)
            dve.wait_ge(tabs_copied, n)
            v.memset(prev_last[:, 0:1], -1.0)
            v.tensor_scalar(last_only[:, 1:2], last_only[:, 0:1], 1.0, None, ALU.subtract).then_inc(setup, 1)
            dve.wait_ge(setup, 3)
            v.tensor_scalar(prev_last[:, 1:NT], dst_col[:, 0:NT - 1], last_only[:, 0:1], last_only[:, 1:2],
                            ALU.mult, ALU.add).then_inc(setup, 1)
            dve.wait_ge(setup, 4)

            def masks(t, u):
                dve.wait_ge(dst_ready, t + 1)
                if not (isinstance(t, int) and t < 2):
                    dve.wait_ge(seg_ready, t - 1)
                v.tensor_scalar(same[:, u % 2, :], ps_dst[u % 2][:, 0:P], dst_col[:, bass.ds(t, 1)], None,
                                ALU.is_equal)
                v.tensor_scalar(carry[:, u % 2, :], ps_dst[u % 2][:, 0:P], prev_last[:, bass.ds(t, 1)], None,
                                ALU.is_equal).then_inc(masks_ready, 1)

            def means(t, u, turn):
                dve.wait_ge(seg_copied, t + 1)
                v.tensor_scalar(deg[:, u:u + 1], seg[:, u, D:D1], 1.0, None, ALU.max).then_inc(deg_ready, 1)
                dve.wait_ge(deg_ready, 2 * t + 1)
                v.reciprocal(rdeg[:, u:u + 1], deg[:, u:u + 1]).then_inc(deg_ready, 1)
                dve.wait_ge(deg_ready, 2 * t + 2)
                if not (isinstance(turn, int) and turn == 0):
                    dve.wait_ge(scattered[u], 16 * turn)
                v.tensor_scalar(mean[:, u, :], seg[:, u, 0:D], rdeg[:, u:u + 1], None,
                                ALU.mult).then_inc(mean_ready, 1)


            def norm(k, groups, parts, chain0):
                xk = xs[:, k & (SL - 1), :]
                ak = ag[:, k & (SL - 1), :]
                at = [0]

                def link(ins):
                    at[0] += 1
                    ins.then_inc(super_chain, 1)
                    dve.wait_ge(super_chain, chain0 + at[0])

                for n, (np_, g0, g1) in enumerate(parts):
                    ins = v.tensor_tensor(xk[0:np_, g0 * D:g1 * D], xk[0:np_, g0 * D:g1 * D],
                                          ak[0:np_, g0 * D:g1 * D], ALU.add)
                link(ins)
                dve.sem_inc(dve_passed, 1)
                for np_, g0, g1 in parts:
                    for g in range(g0, g1):
                        ins = v.bn_stats(stats[0:np_, g, :], xk[0:np_, g * D:(g + 1) * D])
                link(ins)
                a = [tmp[:, j, 0:groups] for j in range(6)]
                st = [stats[:, 0:groups, j] for j in range(6)]
                v.tensor_tensor(a[0], st[1], st[4], ALU.add)
                v.tensor_tensor(a[2], st[2], st[5], ALU.add)
                link(v.tensor_tensor(a[1], st[1], st[4], ALU.subtract))
                link(v.tensor_tensor(a[3], a[1], a[1], ALU.mult))
                link(v.scalar_tensor_tensor(out=a[4], in0=a[3], scalar=D / 4.0, in1=a[2],
                                            op0=ALU.mult, op1=ALU.add))
                v.tensor_scalar(a[4], a[4], 1.0 / D, EPS, ALU.mult, ALU.add).then_inc(var_ready, 1)
                dve.wait_ge(std_ready, k + 1)
                link(v.reciprocal(a[2], a[5]))
                link(v.scalar_tensor_tensor(out=a[3], in0=a[0], scalar=-0.5, in1=a[2],
                                            op0=ALU.mult, op1=ALU.mult))
                for np_, g0, g1 in parts:
                    for g in range(g0, g1):
                        ins = v.tensor_scalar(xk[0:np_, g * D:(g + 1) * D], xk[0:np_, g * D:(g + 1) * D],
                                              tmp[0:np_, 2, g:g + 1], tmp[0:np_, 3, g:g + 1],
                                              ALU.mult, ALU.add)
                ins.then_inc(normed, 1)
                assert at[0] == LINKS

            def supers(c):
                lo = dve.value_load(plan[0:1, 0, bass.ds(c, 1)], min_val=0, max_val=NS)
                hi = dve.value_load(plan[0:1, 0, bass.ds(c + 1, 1)], min_val=0, max_val=NS)
                with dve.If(lo < hi):
                    with dve.Fori(lo, hi) as k:
                        dve.wait_ge(super_loaded, 32 * k + 32)
                        norm(k, G, [(P, 0, G)], LINKS * k)

            masks(0, 0)

            def step(i, last=False):
                for u in range(U):
                    t = i * U + u
                    if not (last and u == U - 1):
                        masks(t + 1, (u + 1) % U)
                    means(t, u, i)
                supers(i)

            dve.wait_ge(plan_ready, 1)
            step(0)
            with dve.Fori(1, NI - 1) as i:
                step(i)
            step(NI - 1, last=True)
            dve.wait_ge(rest_loaded, 64)
            v.memset(stats[:, GR, :], 0.0).then_inc(super_chain, 1)
            dve.wait_ge(super_chain, LINKS * NS + 1)
            norm(NS, GR + 1, [(P, 0, GR), (R1, GR, GR + 1)], LINKS * NS + 1)


_INS = ['x', 'src', 'dst', 'L0_gnn_W', 'L0_gnn_b']


def kernel(**inputs):
    import numpy as _np
    import concourse.bacc as _bacc
    from concourse import mybir as _mybir
    from concourse.bass_utils import run_bass_kernel_spmd as _run
    nc = _bacc.Bacc("TRN2", target_bir_lowering=False, num_devices=1)
    arrays, args = {}, []
    for name in _INS:
        a = _np.ascontiguousarray(inputs[name])
        arrays[f"in_{name}"] = a
        args.append(nc.dram_tensor(f"in_{name}", a.shape, _mybir.dt.from_np(a.dtype), kind="ExternalInput").ap())
    shape = inputs["x"].shape
    args.append(nc.dram_tensor("out_0", tuple(shape), _mybir.dt.float32, kind="ExternalOutput").ap())
    gnn_residual_layernorm(nc, *args)
    r = _run(nc, [arrays], core_ids=[0])
    return r.results[0]["out_0"]
```
